# Optimizing a Trainium2 kernel written in Bass

```python
import numpy as np
import jax
import jax.numpy as jnp

def _softmax(x, axis=-1):
    return jax.nn.softmax(x, axis=axis)

def _gelu(x):
    return jax.nn.gelu(x, approximate=True)

def _silu(x):
    return jax.nn.silu(x)

def _sigmoid(x):
    return jax.nn.sigmoid(x)

def _layernorm(x, axis=-1, eps=1e-05):
    m = jnp.mean(x, axis=axis, keepdims=True)
    v = jnp.var(x, axis=axis, keepdims=True)
    return (x - m) / jnp.sqrt(v + eps)

def _scatter_add(tgt, idx, src, axis=0):
    return tgt.at[idx].add(src)

def _segment_sum(src, seg, n):
    return jax.ops.segment_sum(src, seg, n)
kernel_name = 'mk_gnn_preln_d2_gnn_r32_c60a6b'

def setup_inputs(seed: int=0):
    np.random.seed(seed)
    _w = jnp.asarray

    def _rec_inputs():
        import jax
        import jax.numpy as jnp
        _gk = jax.random.key(seed)
        x = -0.0003713 + 1 * jax.random.normal(jax.random.fold_in(_gk, 1), (3125, 128), jnp.float32)
        src = jax.random.randint(jax.random.fold_in(_gk, 2), (50000,), 0, 3125, jnp.int32)
        dst = jnp.minimum((3125 * jax.random.uniform(jax.random.fold_in(_gk, 3), (50000,)) ** 2.0).astype(jnp.int32), 99999)
        _o = jnp.argsort(dst, stable=True)
        src = src[_o]
        dst = dst[_o]
        return (x, src, dst)
    x, src, dst = _rec_inputs()

    def _L0_gnn_setup():
        import jax, jax.numpy as jnp
        import numpy as np
        N_NODES = 3125
        N_HYPEREDGES = 30000
        N_INC = 9375
        IN_CH = 128
        HID = 256
        OUT_CH = 128
        EPS = 1e-05

        def _hconv(x, node_idx, he_idx, W, b):
            x = x @ W
            ones = jnp.ones((node_idx.shape[0],), x.dtype)
            d = jax.ops.segment_sum(ones, node_idx, num_segments=N_NODES)
            bd = jax.ops.segment_sum(ones, he_idx, num_segments=N_HYPEREDGES)
            Dinv = jnp.where(d > 0, 1.0 / jnp.maximum(d, 1.0), 0.0)
            Binv = jnp.where(bd > 0, 1.0 / jnp.maximum(bd, 1.0), 0.0)
            he = jax.ops.segment_sum(x[node_idx], he_idx, num_segments=N_HYPEREDGES) * Binv[:, None]
            out = jax.ops.segment_sum(he[he_idx], node_idx, num_segments=N_NODES) * Dinv[:, None]
            return out + b

        def _bn(x, g, be):
            m = x.mean(axis=0)
            v = x.var(axis=0)
            return (x - m) * jax.lax.rsqrt(v + EPS) * g + be
        key = jax.random.key(seed)
        ks = jax.random.split(key, 14)
        x = jax.random.normal(ks[0], (N_NODES, IN_CH), jnp.float32)
        node_idx = jax.random.randint(ks[1], (N_INC,), 0, N_NODES)
        he_idx = jax.random.randint(ks[2], (N_INC,), 0, N_HYPEREDGES)
        edge = jnp.stack([node_idx, he_idx], axis=0)
        s1 = 1.0 / np.sqrt(IN_CH)
        s2 = 1.0 / np.sqrt(HID)
        return {'x': x, 'edge': edge, 'W1': jax.random.normal(ks[3], (IN_CH, HID), jnp.float32) * s1, 'b1': jnp.zeros((HID,), jnp.float32), 'g1': jnp.ones((HID,), jnp.float32), 'be1': jnp.zeros((HID,), jnp.float32), 'W2': jax.random.normal(ks[4], (HID, HID), jnp.float32) * s2, 'b2': jnp.zeros((HID,), jnp.float32), 'g2': jnp.ones((HID,), jnp.float32), 'be2': jnp.zeros((HID,), jnp.float32), 'W3': jax.random.normal(ks[5], (HID, OUT_CH), jnp.float32) * s2, 'b3': jnp.zeros((OUT_CH,), jnp.float32)}
    _L0_gnn_all = _L0_gnn_setup()
    _L0_gnn_in = {k: v for k, v in _L0_gnn_all.items() if k in ('W1', 'b1', 'g1', 'be1', 'W2', 'b2', 'g2', 'be2', 'W3', 'b3')}
    del _L0_gnn_all

    def _L1_gnn_setup():
        import jax, jax.numpy as jnp
        import numpy as np
        N = 50000
        E = 25000
        D = 128
        H = 8
        DH = D // H
        L = 2
        LN_EPS = 1e-05

        def layer_norm(x, w, b):
            m = jnp.mean(x, axis=-1, keepdims=True)
            v = jnp.mean((x - m) ** 2, axis=-1, keepdims=True)
            return (x - m) * jax.lax.rsqrt(v + LN_EPS) * w + b
        key = jax.random.key(seed)
        ks = jax.random.split(key, 16)
        s = 0.05

        def nrm(k, shape):
            return jax.random.normal(k, shape, jnp.float32) * s
        inp = {'h': jax.random.normal(ks[0], (N, D), jnp.float32), 'src': jax.random.randint(ks[1], (E,), 0, N), 'dst': jax.random.randint(ks[2], (E,), 0, N), 'W_emb': nrm(ks[3], (D, D)), 'Wq': nrm(ks[4], (L, D, D)), 'bq': jnp.zeros((L, D), jnp.float32), 'Wk': nrm(ks[5], (L, D, D)), 'bk': jnp.zeros((L, D), jnp.float32), 'Wv': nrm(ks[6], (L, D, D)), 'bv': jnp.zeros((L, D), jnp.float32), 'Wo': nrm(ks[7], (L, D, D)), 'bo': jnp.zeros((L, D), jnp.float32), 'ln1_w': jnp.ones((L, D), jnp.float32), 'ln1_b': jnp.zeros((L, D), jnp.float32), 'Wf1': nrm(ks[8], (L, D, 2 * D)), 'bf1': jnp.zeros((L, 2 * D), jnp.float32), 'Wf2': nrm(ks[9], (L, 2 * D, D)), 'bf2': jnp.zeros((L, D), jnp.float32), 'ln2_w': jnp.ones((L, D), jnp.float32), 'ln2_b': jnp.zeros((L, D), jnp.float32)}
        return inp
    _L1_gnn_all = _L1_gnn_setup()
    _L1_gnn_in = {k: v for k, v in _L1_gnn_all.items() if k in ('W_emb', 'Wq', 'bq', 'Wk', 'bk', 'Wv', 'bv', 'Wo', 'bo', 'ln1_w', 'ln1_b', 'Wf1', 'bf1', 'Wf2', 'bf2', 'ln2_w', 'ln2_b')}
    del _L1_gnn_all
    return {'x': x, 'src': src, 'dst': dst, 'L0_gnn_W1': _L0_gnn_in['W1'], 'L0_gnn_b1': _L0_gnn_in['b1'], 'L0_gnn_g1': _L0_gnn_in['g1'], 'L0_gnn_be1': _L0_gnn_in['be1'], 'L0_gnn_W2': _L0_gnn_in['W2'], 'L0_gnn_b2': _L0_gnn_in['b2'], 'L0_gnn_g2': _L0_gnn_in['g2'], 'L0_gnn_be2': _L0_gnn_in['be2'], 'L0_gnn_W3': _L0_gnn_in['W3'], 'L0_gnn_b3': _L0_gnn_in['b3'], 'L1_gnn_W_emb': _L1_gnn_in['W_emb'], 'L1_gnn_Wq': _L1_gnn_in['Wq'], 'L1_gnn_bq': _L1_gnn_in['bq'], 'L1_gnn_Wk': _L1_gnn_in['Wk'], 'L1_gnn_bk': _L1_gnn_in['bk'], 'L1_gnn_Wv': _L1_gnn_in['Wv'], 'L1_gnn_bv': _L1_gnn_in['bv'], 'L1_gnn_Wo': _L1_gnn_in['Wo'], 'L1_gnn_bo': _L1_gnn_in['bo'], 'L1_gnn_ln1_w': _L1_gnn_in['ln1_w'], 'L1_gnn_ln1_b': _L1_gnn_in['ln1_b'], 'L1_gnn_Wf1': _L1_gnn_in['Wf1'], 'L1_gnn_bf1': _L1_gnn_in['bf1'], 'L1_gnn_Wf2': _L1_gnn_in['Wf2'], 'L1_gnn_bf2': _L1_gnn_in['bf2'], 'L1_gnn_ln2_w': _L1_gnn_in['ln2_w'], 'L1_gnn_ln2_b': _L1_gnn_in['ln2_b']}

def reference(x, src, dst, L0_gnn_W1, L0_gnn_b1, L0_gnn_g1, L0_gnn_be1, L0_gnn_W2, L0_gnn_b2, L0_gnn_g2, L0_gnn_be2, L0_gnn_W3, L0_gnn_b3, L1_gnn_W_emb, L1_gnn_Wq, L1_gnn_bq, L1_gnn_Wk, L1_gnn_bk, L1_gnn_Wv, L1_gnn_bv, L1_gnn_Wo, L1_gnn_bo, L1_gnn_ln1_w, L1_gnn_ln1_b, L1_gnn_Wf1, L1_gnn_bf1, L1_gnn_Wf2, L1_gnn_bf2, L1_gnn_ln2_w, L1_gnn_ln2_b):
    import jax
    import jax.numpy as jnp

    def _L0_gnn_ref(x, edge, W1, b1, g1, be1, W2, b2, g2, be2, W3, b3):
        import jax, jax.numpy as jnp
        import numpy as np
        N_NODES = 3125
        N_HYPEREDGES = 30000
        N_INC = 9375
        IN_CH = 128
        HID = 256
        OUT_CH = 128
        EPS = 1e-05

        def _hconv(x, node_idx, he_idx, W, b):
            x = x @ W
            ones = jnp.ones((node_idx.shape[0],), x.dtype)
            d = jax.ops.segment_sum(ones, node_idx, num_segments=N_NODES)
            bd = jax.ops.segment_sum(ones, he_idx, num_segments=N_HYPEREDGES)
            Dinv = jnp.where(d > 0, 1.0 / jnp.maximum(d, 1.0), 0.0)
            Binv = jnp.where(bd > 0, 1.0 / jnp.maximum(bd, 1.0), 0.0)
            he = jax.ops.segment_sum(x[node_idx], he_idx, num_segments=N_HYPEREDGES) * Binv[:, None]
            out = jax.ops.segment_sum(he[he_idx], node_idx, num_segments=N_NODES) * Dinv[:, None]
            return out + b

        def _bn(x, g, be):
            m = x.mean(axis=0)
            v = x.var(axis=0)
            return (x - m) * jax.lax.rsqrt(v + EPS) * g + be
        node_idx = edge[0]
        he_idx = edge[1]
        h = _bn(jax.nn.relu(_hconv(x, node_idx, he_idx, W1, b1)), g1, be1)
        h = _bn(jax.nn.relu(_hconv(h, node_idx, he_idx, W2, b2)), g2, be2)
        h = jax.nn.relu(_hconv(h, node_idx, he_idx, W3, b3))
        return h

    def _L1_gnn_ref(h, src, dst, W_emb, Wq, bq, Wk, bk, Wv, bv, Wo, bo, ln1_w, ln1_b, Wf1, bf1, Wf2, bf2, ln2_w, ln2_b):
        import jax, jax.numpy as jnp
        import numpy as np
        N = 50000
        E = 25000
        D = 128
        H = 8
        DH = D // H
        L = 2
        LN_EPS = 1e-05

        def layer_norm(x, w, b):
            m = jnp.mean(x, axis=-1, keepdims=True)
            v = jnp.mean((x - m) ** 2, axis=-1, keepdims=True)
            return (x - m) * jax.lax.rsqrt(v + LN_EPS) * w + b
        n = h.shape[0]
        scale = 1.0 / np.sqrt(DH)
        h = h @ W_emb
        for l in range(L):
            q = (h @ Wq[l] + bq[l]).reshape(n, H, DH)
            k = (h @ Wk[l] + bk[l]).reshape(n, H, DH)
            v = (h @ Wv[l] + bv[l]).reshape(n, H, DH)
            s = jnp.einsum('ehd,ehd->eh', k[src], q[dst]) * scale
            s = jnp.exp(jnp.clip(s, -5.0, 5.0))
            wV = jax.ops.segment_sum(v[src] * s[:, :, None], dst, num_segments=n)
            z = jax.ops.segment_sum(s, dst, num_segments=n)
            attn = (wV / (z[:, :, None] + 1e-06)).reshape(n, D)
            hx = layer_norm(h + attn @ Wo[l] + bo[l], ln1_w[l], ln1_b[l])
            ffn = jax.nn.relu(hx @ Wf1[l] + bf1[l]) @ Wf2[l] + bf2[l]
            h = layer_norm(hx + ffn, ln2_w[l], ln2_b[l])
        return h
    edge_index = jnp.stack([src, dst])
    h = jnp.maximum(_layernorm(x, axis=-1), 0.0)
    x = x + _L0_gnn_ref(h, edge_index, L0_gnn_W1, L0_gnn_b1, L0_gnn_g1, L0_gnn_be1, L0_gnn_W2, L0_gnn_b2, L0_gnn_g2, L0_gnn_be2, L0_gnn_W3, L0_gnn_b3)
    h = jnp.maximum(_layernorm(x, axis=-1), 0.0)
    x = x + _L1_gnn_ref(h, src, dst, L1_gnn_W_emb, L1_gnn_Wq, L1_gnn_bq, L1_gnn_Wk, L1_gnn_bk, L1_gnn_Wv, L1_gnn_bv, L1_gnn_Wo, L1_gnn_bo, L1_gnn_ln1_w, L1_gnn_ln1_b, L1_gnn_Wf1, L1_gnn_bf1, L1_gnn_Wf2, L1_gnn_bf2, L1_gnn_ln2_w, L1_gnn_ln2_b)
    return x

_drawn_inputs = setup_inputs


def setup_inputs(seed=0):
    import zlib

    import numpy as np

    out = dict(_drawn_inputs(seed))
    spreads = {'L0_gnn_b1': (0.0, 0.1),
     'L0_gnn_g1': (1.0, 0.6),
     'L0_gnn_be1': (0.0, 0.278),
     'L0_gnn_b2': (0.0, 0.272),
     'L0_gnn_g2': (1.0, 0.6),
     'L0_gnn_be2': (0.0, 0.1),
     'L0_gnn_b3': (0.0, 0.1),
     'L1_gnn_bq': (0.0, 0.8),
     'L1_gnn_bk': (0.0, 0.8),
     'L1_gnn_bv': (0.0, 0.1),
     'L1_gnn_bo': (0.0, 0.1),
     'L1_gnn_ln1_w': (1.0, 0.2),
     'L1_gnn_ln1_b': (0.0, 0.1),
     'L1_gnn_bf1': (0.0, 0.1),
     'L1_gnn_bf2': (0.0, 0.1),
     'L1_gnn_ln2_w': (1.0, 0.2),
     'L1_gnn_ln2_b': (0.0, 0.1)}
    factors = {'L1_gnn_Wq': 4.217, 'L1_gnn_Wk': 4.039}
    for name, (base, spread) in spreads.items():
        noise = np.random.default_rng([zlib.crc32(name.encode()), seed]).standard_normal(out[name].shape)
        drawn = base * np.exp(spread * noise) if base else spread * noise
        out[name] = jnp.asarray(drawn.astype(out[name].dtype))
    for name, factor in factors.items():
        out[name] = (out[name] * factor).astype(out[name].dtype)
    return out
```

```python
import concourse.bass as bass
from concourse import mybir
from contextlib import ExitStack

N, E, D, HID, H, LAYERS = 3125, 50000, 128, 256, 8, 2
P = 128
NT = -(-N // P)
LAST = N - (NT - 1) * P
NP = NT * P
EC = 392
FULL = E // EC
REST = E - FULL * EC
CH = 8
RING = 4
T = 416
CHUNKS = T // CH
SPAN = RING * CH
SLOTS = T * P
DUMP = EC * P - E
SC = 14
GW = 264
AW = 256
EMPTY = 255
LN_EPS = 1e-5
CLIP = 5.0 * (D // H) ** 0.5
SCALE = (D // H) ** -0.5

ALU = mybir.AluOpType
ACT = mybir.ActivationFunctionType
AX = mybir.AxisListType
f32, i32, bf16 = mybir.dt.float32, mybir.dt.int32, mybir.dt.bfloat16

BY_DST, BY_SRC = 0, 1
PASSES = [(BY_DST, "t_h0", 128, 129), (BY_SRC, "t_e1", 128, 129), (BY_DST, "t_h1", 256, 256),
          (BY_SRC, "t_e2", 256, 256), (BY_DST, "t_x3", 128, 128), (BY_SRC, "t_e3", 128, 128),
          (BY_DST, "t_kv0", 256, 136), (BY_DST, "t_kv1", 256, 136)]
TABLES = {name: width for _, name, width, _ in PASSES}

QUADS = [list(range(a, min(a + 4, NT))) for a in range(0, NT, 4)]
PAIRS = [list(range(a, min(a + 2, NT))) for a in range(0, NT, 2)]
SPANS = [(a, min(512, NP - a)) for a in range(0, NP, 512)]
_PHASES = [("z1", 7), ("w1", 14), ("t2", 13), ("r2", 13), ("x3", 7), ("h", 7), ("emb", 7), ("embT", 7)]
for _l in range(LAYERS):
    _PHASES += [(f"qkv{_l}", NT), (f"at{_l}", 7), (f"wo{_l}", 7), (f"hx{_l}", 7), (f"f1{_l}", 14), (f"f2{_l}", 7)]
    if _l + 1 < LAYERS:
        _PHASES += [(f"nx{_l}", 7)]
FIRST = {}
_n = 0
for _name, _count in _PHASES:
    FIRST[_name] = _n
    _n += _count


def build(nc, x, src, dst, W1, b1, g1, be1, W2, b2, g2, be2, W3, b3, Wemb, Wq, bq, Wk, bk, Wv, bv, Wo, bo,
          l1w, l1b, Wf1, bf1, Wf2, bf2, l2w, l2b, out):
    ctx = ExitStack()
    with ctx:
        def sb(name, shape, dt=f32):
            return ctx.enter_context(nc.sbuf_tensor(name, shape, dt))

        def sem(name):
            return ctx.enter_context(nc.semaphore(name))

        ctx.enter_context(nc.allow_non_contiguous_dma(reason="per-partition biases"))
        slots_d = [nc.dram_tensor(f"slots{o}_dram", (SLOTS + DUMP, 2), i32, kind="Internal").ap() for o in range(2)]
        table = {n: nc.dram_tensor(n + "_dram", (NP, w), f32, kind="Internal").ap() for n, w in TABLES.items()}

        iota_i = sb("iota_i", [P, P], i32)
        part_i = sb("part_i", [P, 1], i32)
        tile_i = sb("tile_i", [P, T], i32)
        iota = sb("iota", [P, P])
        part = sb("part", [P, 1])
        ident = sb("ident", [P, P])
        below = sb("below", [P, P])
        ones = sb("ones", [P, P])
        gidx = [sb(f"gidx{o}", [P, T], i32) for o in range(2)]
        local = [sb(f"local{o}", [P, T]) for o in range(2)]
        acc_at = [sb(f"acc_at{o}", [1, T], i32) for o in range(2)]
        q_at = sb("q_at", [1, T], i32)
        slotmap = sb("slotmap", [P, T * 2], i32)
        stage_idx = sb("stage_idx", [P, 2, SC], i32)
        stage_pay = sb("stage_pay", [P, 2, SC * 2], i32)
        idx_ring = sb("idx_ring", [P, RING * CH], i32)
        G = sb("G", [P, RING * CH, GW])
        onehot = sb("onehot", [P, 2 * CH, P])
        onehotT = sb("onehotT", [P, CH, P])
        acc = sb("acc", [P, NT, AW])
        tab = sb("tab", [P, NT, 256])
        wide = sb("wide", [P, 25 * EC])
        xres = sb("xres", [P, NT, D])
        h = sb("h", [P, NT, D])
        small = sb("small", [P, 8, 32])
        small_i = sb("small_i", [P, 32], i32)
        inv = [sb(f"inv{o}", [P, NT]) for o in range(2)]
        z_inv = sb("z_inv", [P, NT, H])
        stats = sb("stats", [P, 2, 7, 6])
        mv = sb("mv", [P, 2, 2])
        bn = sb("bn", [P, 4, 2])
        W1_s = sb("W1_s", [P, HID])
        W2_s = sb("W2_s", [P, 2, HID])
        W3_s = sb("W3_s", [P, 2, D])
        Wemb_s = sb("Wemb_s", [P, D])
        cols = sb("cols", [P, 5, 2])
        rows = sb("rows", [P, HID + D])
        Wqkv_s = [sb(f"Wqkv_s{l}", [P, 3, D]) for l in range(LAYERS)]
        Wo_s = [sb(f"Wo_s{l}", [P, D]) for l in range(LAYERS)]
        Wf1_s = [sb(f"Wf1_s{l}", [P, 2 * D]) for l in range(LAYERS)]
        Wf2_s = [sb(f"Wf2_s{l}", [P, 2, D]) for l in range(LAYERS)]
        bf1_s = [sb(f"bf1_s{l}", [P, 2]) for l in range(LAYERS)]
        lrow = [sb(f"lrow{l}", [P, 9, D]) for l in range(LAYERS)]
        mask = tab[:].rearrange("p a b -> p (a b)").bitcast(bf16)[:, 0:NT * EC].rearrange("p (b c) -> p b c", c=EC)
        cum = wide[:, 0:NT * EC].rearrange("p (b c) -> p b c", c=EC)
        hflat = h[:].rearrange("p a b -> p (a b)")
        accflat = acc[:].rearrange("p a b -> p (a b)")
        key_i = [accflat[:, o * EC:(o + 1) * EC].bitcast(i32) for o in range(2)]
        blk_i = accflat[:, 2 * EC:3 * EC].bitcast(i32)
        blk = accflat[:, 3 * EC:4 * EC]
        zeros = accflat[:, 4 * EC:5 * EC]
        padpos = accflat[:, 5 * EC:6 * EC]
        pos = accflat[:, 6 * EC:7 * EC]
        pos_hi = accflat[:, 7 * EC:8 * EC].bitcast(i32)
        edge_i = accflat[:, 8 * EC:9 * EC].bitcast(i32)
        pos_s = accflat[:, 9 * EC:10 * EC].bitcast(i32)
        bt = accflat[:, 10 * EC:10 * EC + T]
        pos_i = [hflat[:, o * EC:(o + 1) * EC].bitcast(i32) for o in range(2)]
        pay = [hflat[:, (2 + 2 * o) * EC:(4 + 2 * o) * EC].bitcast(i32).rearrange("p (c two) -> p c two", two=2)
               for o in range(2)]
        zT = wide[:, 0:NP]
        hT = wide[:, NP:3 * NP].rearrange("p (o n) -> p o n", o=2)
        sT = wide[:, NP:2 * NP]
        q = wide[:, 2 * NP:3 * NP]

        PB = ctx.enter_context(nc.psum_tensor("PB", [P, 8, 512], f32))
        sums = PB[:, 0:4, :].rearrange("p b (two w) -> p (b two) w", two=2)
        q_edge = PB[:, 4:6, :].rearrange("p b (k w) -> p (b k) w", w=P)
        ohT_ps = PB[:, 6:8, :].rearrange("p b (k w) -> p (b k) w", w=P)

        loaded_edges, loaded_x, loaded_w = sem("loaded_edges"), sem("loaded_x"), sem("loaded_w")
        prefilled = sem("prefilled")
        pool_const, dve_chain, act_chain = sem("pool_const"), sem("dve_chain"), sem("act_chain")
        consts_ready = sem("consts_ready")
        x_zeroed, keys_padded, fill_ready = sem("x_zeroed"), sem("keys_padded"), sem("fill_ready")
        counted, counts_summed = sem("counted"), sem("counts_summed")
        pos_ready = sem("pos_ready")
        staged = sem("staged")
        scattered = [sem(f"scattered{i}") for i in range(2)]
        slots_back = sem("slots_back")
        slots_split = sem("slots_split")
        idx_staged = sem("idx_staged")
        gathered = [sem(f"gathered{i}") for i in range(RING)]
        onehot_ready = sem("onehot_ready")
        tile_summed = sem("tile_summed")
        tile_added = sem("tile_added")
        ohT_in_psum, ohT_ready, q_rows = sem("ohT_in_psum"), sem("ohT_ready"), sem("q_rows")
        scored, s_chain, clipped, weighted, messages = (sem("scored"), sem("s_chain"), sem("clipped"),
                                                        sem("weighted"), sem("messages"))
        tab_ready = sem("tab_ready")
        tab_written = [sem(f"tab_written{i}") for i in range(8)]
        group_ready = sem("group_ready")
        bank_free = [sem(f"bank_free{i}") for i in range(4)]
        act_needs = sem("act_needs")
        act_done = sem("act_done")
        mm_input = sem("mm_input")
        ones_col = sem("ones_col")
        final_ready, out_written = sem("final_ready"), sem("out_written")
        block = ctx.enter_context(nc.Block())

        def bank(n):
            return PB[:, 4 + n % 4, :]

        def wait_filled(eng, n):
            eng.wait_ge(group_ready, n + 1)

        def wait_evacuated(eng, n):
            eng.wait_ge(bank_free[n % 4], n // 4 + 1)

        def wait_phase(eng, name, count):
            for n in range(FIRST[name] + max(0, count - 4), FIRST[name] + count):
                wait_evacuated(eng, n)

        def bcast(ap, n):
            return ap.unsqueeze(2).to_broadcast([ap.shape[0], ap.shape[1], n])

        def rowcast(ap, n):
            return ap.unsqueeze(1).to_broadcast([ap.shape[0], n, ap.shape[1]])

        nodes = lambda t: t.rearrange("(j p) c -> p j c", p=P)

        @block.sync
        def _(sp):
            sp.wait_ge(keys_padded, 1)
            for key, o in ((dst, 0), (src, 1)):
                sp.dma_start(key_i[o][0:FULL, :], key[0:FULL * EC].rearrange("(p c) -> p c", c=EC)).then_inc(loaded_edges, 16)
                sp.dma_start(key_i[o][FULL:FULL + 1, 0:REST], key[FULL * EC:E].rearrange("(p c) -> p c", p=1)).then_inc(loaded_edges, 16)
            sp.wait_ge(x_zeroed, 1)
            sp.dma_start(xres[:, 0:NT - 1, :], x[0:(NT - 1) * P, :].rearrange("(j p) c -> p j c", p=P)).then_inc(loaded_x, 16)
            sp.dma_start(xres[0:LAST, NT - 1, :], x[(NT - 1) * P:N, :]).then_inc(loaded_x, 16)
            sp.wait_ge(fill_ready, 1)
            for o in range(2):
                sp.dma_start(slots_d[o][0:SLOTS, :].rearrange("(p t) two -> p (t two)", p=P), slotmap[:, :]).then_inc(prefilled, 16)
            def load(dst_ap, src_ap):
                sp.dma_start(dst_ap, src_ap).then_inc(loaded_w, 16)

            load(W1_s[:], W1)
            load(W2_s[:], W2.rearrange("(k p) c -> p k c", p=P))
            load(W3_s[:], W3.rearrange("(k p) c -> p k c", p=P))
            load(Wemb_s[:], Wemb)
            for i, v in enumerate((b1, g1, be1, g2, be2)):
                load(cols[:, i, :], v.rearrange("(o p) -> p o", p=P))
            load(rows[:, 0:HID], b2.partition_broadcast(P))
            load(rows[:, HID:HID + D], b3.partition_broadcast(P))
            for l in range(LAYERS):
                for i, w in enumerate((Wq, Wk, Wv)):
                    load(Wqkv_s[l][:, i, :], w[l])
                load(Wo_s[l][:], Wo[l])
                load(Wf1_s[l][:], Wf1[l])
                load(Wf2_s[l][:], Wf2[l].rearrange("(k p) c -> p k c", p=P))
                load(bf1_s[l][:], bf1[l].rearrange("(o p) -> p o", p=P))
                for i, v in enumerate((bq, bk, bv, bo, l1w, l1b, bf2, l2w, l2b)):
                    load(lrow[l][:, i, :], v[l].partition_broadcast(P))

            def write_table(i):
                _, name, w, _ = PASSES[i]
                sp.wait_ge(tab_ready, i + 1)
                sp.dma_start(nodes(table[name]), tab[:, :, 0:w]).then_inc(tab_written[i], 16)

            for o in range(2):
                for half in range(2):
                    sp.wait_ge(scattered[half], (o + 1) * EC // 2 * 16)
                if o:
                    sp.wait_ge(slots_split, 1)
                else:
                    sp.wait_ge(prefilled, 32)
                sp.dma_start(slotmap[:, :], slots_d[o][0:SLOTS, :].rearrange("(p t) two -> p (t two)", p=P)).then_inc(slots_back, 16)
                if not o:
                    write_table(0)
            for i in range(1, 8):
                write_table(i)
            sp.wait_ge(final_ready, 1)
            sp.dma_start(out[0:(NT - 1) * P, :].rearrange("(j p) c -> p j c", p=P), h[:, 0:NT - 1, :]).then_inc(out_written, 16)
            sp.dma_start(out[(NT - 1) * P:N, :], h[0:LAST, NT - 1, :]).then_inc(out_written, 16)
            sp.wait_ge(out_written, 32)
            for i in range(8):
                sp.wait_ge(tab_written[i], 16)

        @block.gpsimd
        def _(pool):
            nc.gpsimd.iota(iota_i[:], [[1, P]], base=0, channel_multiplier=0).then_inc(pool_const, 1)
            nc.gpsimd.iota(part_i[:], [[0, 1]], base=0, channel_multiplier=1).then_inc(pool_const, 1)
            nc.gpsimd.iota(edge_i, [[1, EC]], base=0, channel_multiplier=EC).then_inc(pool_const, 1)
            nc.gpsimd.iota(tile_i[:], [[1, T]], base=0, channel_multiplier=0).then_inc(pool_const, 1)
            nc.gpsimd.memset(G[:, :, D:D + 1], 1.0).then_inc(ones_col, 1)
            for o in range(2):
                with pool.Fori(0, EC // (2 * SC)) as turn:
                    c = turn * (2 * SC)
                    for half in range(2):
                        pool.wait_ge(staged, c + (o * EC + (half + 1) * SC))
                        pool.nop(nofuse=True)
                        pool.wait_ge(prefilled, 32)
                        for k in range(SC):
                            pool.indirect_dma_start(
                                slots_d[o], bass.IndirectOffsetOnAxis(ap=stage_idx[:, half, k:k + 1], axis=0),
                                stage_pay[:, half, 2 * k:2 * k + 2], None).then_inc(scattered[half], 16)
            for p, (order, name, w, _) in enumerate(PASSES):
                with pool.Fori(0, T // SPAN) as turn:
                    t = turn * SPAN
                    for c in range(RING):
                        pool.wait_ge(idx_staged, t + (p * T + (c + 1) * CH))
                        pool.nop(nofuse=True)
                        pool.wait_ge(tab_written[p], 16)
                        for k in range(c * CH, (c + 1) * CH):
                            pool.indirect_dma_start(
                                G[:, k, 0:w], None, table[name],
                                bass.IndirectOffsetOnAxis(ap=idx_ring[:, k:k + 1], axis=0)).then_inc(gathered[c], 16)

        @block.scalar
        def _(act):
            links = [0]

            def link(ins):
                links[0] += 1
                ins.then_inc(act_chain, 1)
                act.wait_ge(act_chain, links[0])

            needs = [0]

            def wait_dve():
                needs[0] += 1
                act.wait_ge(act_needs, needs[0])

            def stage_scatter(o, c, first=False):
                for half in range(2):
                    if not first:
                        act.wait_ge(scattered[half], c * 8 + o * EC * 8)
                    nc.scalar.activation(stage_idx[:, half, :], pos_i[o][:, bass.ds(c + half * SC, SC)], ACT.Copy)
                    nc.scalar.activation(stage_pay[:, half, :],
                                         pay[o].rearrange("p c two -> p (c two)")[:, bass.ds(c * 2 + half * SC * 2, 2 * SC)],
                                         ACT.Copy).then_inc(staged, SC)

            for o in range(2):
                act.wait_ge(pos_ready, o + 1)
                if o == 0:
                    stage_scatter(0, 0, first=True)
                with act.Fori(1 - o, EC // (2 * SC)) as turn:
                    stage_scatter(o, turn * (2 * SC))

            def stage_indices(p, c, t):
                act.wait_ge(tile_summed, t + (p * T + CH))
                nc.scalar.activation(idx_ring[:, c * CH:(c + 1) * CH], gidx[PASSES[p][0]][:, bass.ds(t, CH)],
                                     ACT.Copy).then_inc(idx_staged, CH)

            def simple_pass(p):
                with act.Fori(0, T // SPAN) as turn:
                    t = turn * SPAN
                    for c in range(RING):
                        stage_indices(p, c, t + c * CH)

            def evacuate(n, dst_ap, src_ap, func=ACT.Copy, **kw):
                wait_filled(act, n)
                nc.scalar.activation(dst_ap, src_ap, func, **kw).then_inc(bank_free[n % 4], 1)

            def evacuate_transposed(name, dst_ap):
                for g, tiles in enumerate(QUADS):
                    m = len(tiles) * P
                    evacuate(FIRST[name] + g, dst_ap[:, tiles[0] * P:tiles[0] * P + m], bank(FIRST[name] + g)[:, 0:m])

            wait_dve()
            nc.scalar.activation(small[:, 3, 0:NT], small[:, 2, 0:NT], ACT.Sqrt).then_inc(act_done, 1)
            act.wait_ge(slots_split, 1)
            simple_pass(0)
            act.wait_ge(slots_split, 2)
            simple_pass(1)
            act.wait_ge(loaded_w, 16 * WEIGHT_LOADS)
            evacuate_transposed("z1", zT)
            for i, (o, (a, m)) in enumerate((o, s) for o in range(2) for s in SPANS):
                n = FIRST["w1"] + i
                evacuate(n, hT[:, o, a:a + m], bank(n)[:, 0:m], ACT.Relu, bias=cols[:, 0, o:o + 1])
            wait_dve()
            nc.scalar.activation(bn[:, 1, :], bn[:, 0, :], ACT.Sqrt).then_inc(act_done, 1)
            for g, tiles in enumerate(PAIRS):
                n = FIRST["t2"] + g
                evacuate(n, tab[:, tiles[0]:tiles[-1] + 1, :],
                         bank(n)[:, 0:len(tiles) * 256].rearrange("p (j c) -> p j c", c=256))
            simple_pass(2)
            simple_pass(3)
            for g, tiles in enumerate(PAIRS):
                n, m = FIRST["r2"] + g, len(tiles) * P
                evacuate(n, hT[:, :, tiles[0] * P:tiles[0] * P + m],
                         bank(n)[:, 0:2 * m].rearrange("p (o n) -> p o n", o=2))
            wait_dve()
            nc.scalar.activation(bn[:, 1, :], bn[:, 0, :], ACT.Sqrt).then_inc(act_done, 1)
            for g, tiles in enumerate(QUADS):
                n = FIRST["x3"] + g
                evacuate(n, tab[:, tiles[0]:tiles[-1] + 1, 0:D],
                         bank(n)[:, 0:len(tiles) * P].rearrange("p (j c) -> p j c", c=P))
            simple_pass(4)
            simple_pass(5)

            def root():
                wait_dve()
                nc.scalar.activation(small[:, 3, 0:NT], small[:, 2, 0:NT], ACT.Sqrt).then_inc(act_done, 1)

            root()
            evacuate_transposed("h", zT)
            for g, tiles in enumerate(QUADS):
                n = FIRST["emb"] + g
                evacuate(n, h[:, tiles[0]:tiles[-1] + 1, :],
                         bank(n)[:, 0:len(tiles) * P].rearrange("p (j c) -> p j c", c=P))
            evacuate_transposed("embT", sT)
            for l in range(LAYERS):
                p = 6 + l
                base = l * T

                def copy_onehotT(t):
                    act.wait_ge(ohT_in_psum, t + (base + CH))
                    if not (l == 0 and isinstance(t, int) and t == 0):
                        act.wait_ge(q_rows, t + base)
                    nc.scalar.activation(onehotT[:], ohT_ps, ACT.Copy).then_inc(ohT_ready, CH)

                def weigh(t, c):
                    act.wait_ge(clipped, t + (base + CH))
                    s = G[:, c * CH:(c + 1) * CH, 2 * D:2 * D + H]
                    nc.scalar.activation(s, s, ACT.Exp, scale=SCALE).then_inc(weighted, CH)

                for c in range(3):
                    stage_indices(p, c, c * CH)
                copy_onehotT(0)

                def step(t, c, ahead=True, more=True):
                    if ahead:
                        stage_indices(p, (c + 3) % RING, t + 3 * CH)
                    if more:
                        copy_onehotT(t + CH)
                    weigh(t, c)

                step(0, 0)
                with act.Fori(0, (T - SPAN) // SPAN) as turn:
                    t = turn * SPAN
                    for k in range(1, RING + 1):
                        step(t + k * CH, k % RING)
                step(T - 3 * CH, 1, ahead=False)
                step(T - 2 * CH, 2, ahead=False)
                step(T - CH, 3, ahead=False, more=False)
                evacuate_transposed(f"at{l}", zT)
                root()
                evacuate_transposed(f"hx{l}", zT)
                for i, (o, (a, m)) in enumerate((o, s) for o in range(2) for s in SPANS):
                    n = FIRST[f"f1{l}"] + i
                    evacuate(n, hT[:, o, a:a + m], bank(n)[:, 0:m], ACT.Relu, bias=bf1_s[l][:, o:o + 1])
                root()
                if l + 1 < LAYERS:
                    evacuate_transposed(f"nx{l}", sT)

        @block.vector
        def _(dve):
            links = [0]

            def link(ins):
                links[0] += 1
                ins.then_inc(dve_chain, 1)
                dve.wait_ge(dve_chain, links[0])

            acts = [0]

            def wait_act():
                acts[0] += 1
                dve.wait_ge(act_done, acts[0])

            V = nc.vector
            V.memset(key_i[0], NP)
            V.memset(key_i[1], NP).then_inc(keys_padded, 1)
            V.memset(xres[:, NT - 1, :], 0.0).then_inc(x_zeroed, 1)
            sm3 = slotmap[:].rearrange("p (t two) -> p t two", two=2)
            V.memset(sm3[:, :, 0], 0)
            V.memset(sm3[:, :, 1], EMPTY).then_inc(fill_ready, 1)
            V.memset(zeros, 0.0)
            link(V.memset(ones[:], 1.0))
            dve.wait_ge(pool_const, 4)
            V.tensor_copy(iota[:], iota_i[:])
            V.tensor_copy(bt, tile_i[:])
            V.tensor_copy(padpos, edge_i)
            link(V.tensor_copy(part[:], part_i[:]))
            V.tensor_scalar(ident[:], iota[:], part[:, 0:1], None, ALU.is_equal)
            link(V.tensor_scalar(below[:], iota[:], part[:, 0:1], None, ALU.is_gt))
            link(V.tensor_scalar(pos, padpos, float(E), None, ALU.is_ge))
            link(V.tensor_scalar(padpos, padpos, float(SLOTS - E), None, ALU.add))
            V.tensor_tensor(padpos, padpos, pos, ALU.mult).then_inc(consts_ready, 1)
            dve.wait_ge(consts_ready, 1)
            dve.wait_ge(loaded_edges, 64)

            for o in range(2):
                key, other = key_i[o], key_i[1 - o]
                link(V.tensor_scalar(blk_i, key, 7, None, ALU.logical_shift_right))
                V.tensor_copy(pay[o][:, :, 0], other)
                V.tensor_scalar(pos_s, key, P - 1, None, ALU.bitwise_and)
                link(V.tensor_copy(blk, blk_i))
                V.tensor_copy(pay[o][:, :, 1], pos_s)
                for b in range(NT):
                    link(V.tensor_scalar(mask[:, b, :], blk, float(b), None, ALU.is_equal))
                    ins = V.tensor_tensor_scan(cum[:, b, :], mask[:, b, :], zeros, 0.0, ALU.add, ALU.add)
                link(ins)
                V.tensor_copy(small[:, 0, 0:NT], cum[:, :, EC - 1]).then_inc(counted, 1)
                dve.wait_ge(counts_summed, o + 1)
                before, total = PB[:, 7, 0:NT], PB[:, 7, 64:64 + NT]
                link(V.tensor_scalar(small_i[:, 0:NT], total, float(P - 1), None, ALU.add))
                link(V.tensor_scalar(small_i[:, 0:NT], small_i[:, 0:NT], 7, None, ALU.logical_shift_right))
                link(V.tensor_copy(small[:, 1, 0:NT], small_i[:, 0:NT]))
                link(V.tensor_tensor_scan(small[:, 2, 0:NT], small[:, 1, 0:NT], zeros[:, 0:NT], 0.0, ALU.add, ALU.add))
                link(V.tensor_tensor(small[:, 3, 0:NT], small[:, 2, 0:NT], small[:, 1, 0:NT], ALU.subtract))
                link(V.tensor_scalar(small[:, 3, 0:NT], small[:, 3, 0:NT], float(P), -1.0, ALU.mult, ALU.add))
                link(V.tensor_tensor(small[:, 3, 0:NT], before, small[:, 3, 0:NT], ALU.add))
                link(V.tensor_tensor(cum, cum, bcast(small[:, 3, 0:NT], EC), ALU.add))
                link(V.tensor_tensor(cum, cum, mask, ALU.mult))
                link(V.tensor_reduce(pos, cum.rearrange("p b c -> p c b"), AX.X, ALU.add))
                link(V.tensor_copy(pos_s, pos))
                link(V.tensor_scalar(pos_hi, pos_s, 7, None, ALU.logical_shift_right))
                link(V.tensor_scalar(pos_s, pos_s, P - 1, None, ALU.bitwise_and))
                link(V.tensor_copy(blk, pos_hi))
                link(V.tensor_copy(pos, pos_s))
                link(V.scalar_tensor_tensor(pos, pos, float(T), blk, ALU.mult, ALU.add))
                link(V.tensor_tensor(pos, pos, padpos, ALU.add))
                V.tensor_copy(pos_i[o], pos).then_inc(pos_ready, 1)
                tb = [onehot[:, 0:4, :].rearrange("p a b -> p (a b)")[:, 0:T],
                      onehot[:, 4:8, :].rearrange("p a b -> p (a b)")[:, 0:T]]
                link(V.memset(tb[0], 0.0))
                for b in range(NT):
                    link(V.scalar_tensor_tensor(tb[(b + 1) % 2], bt, small[:, 2, b:b + 1], tb[b % 2], ALU.is_ge, ALU.add))
                link(V.tensor_scalar(tb[(NT + 1) % 2], tb[NT % 2], float(NT - 1), float(AW), ALU.min, ALU.mult))
                link(V.tensor_copy(acc_at[o][0:1, :], tb[(NT + 1) % 2][0:1, :]))
                if o == BY_DST:
                    link(V.tensor_scalar(tb[0], tb[(NT + 1) % 2], D / AW, None, ALU.mult))
                    link(V.tensor_copy(q_at[0:1, :], tb[0][0:1, :]))

            def layer_norm(t, scratch, weight=None, bias=None, relu=False):
                link(V.tensor_reduce(small[:, 0, 0:NT], t, AX.X, ALU.add))
                link(V.tensor_scalar(small[:, 0, 0:NT], small[:, 0, 0:NT], 1.0 / D, None, ALU.mult))
                link(V.tensor_tensor(t, t, bcast(small[:, 0, 0:NT], D), ALU.subtract))
                link(V.tensor_tensor(scratch, t, t, ALU.mult))
                link(V.tensor_reduce(small[:, 1, 0:NT], scratch, AX.X, ALU.add))
                V.tensor_scalar(small[:, 2, 0:NT], small[:, 1, 0:NT], 1.0 / D, LN_EPS, ALU.mult, ALU.add).then_inc(act_needs, 1)
                wait_act()
                link(V.reciprocal(small[:, 4, 0:NT], small[:, 3, 0:NT]))
                link(V.tensor_tensor(t, t, bcast(small[:, 4, 0:NT], D), ALU.mult))
                if weight is not None:
                    link(V.tensor_tensor(t, t, rowcast(weight, NT), ALU.mult))
                    link(V.tensor_tensor(t, t, rowcast(bias, NT), ALU.add))
                if relu:
                    link(V.tensor_scalar(t, t, 0.0, None, ALU.max))

            dve.wait_ge(loaded_x, 32)
            t0 = tab[:, :, 0:D]
            link(V.tensor_copy(t0, xres[:]))
            layer_norm(t0, wide[:, 0:NP].rearrange("p (j c) -> p j c", c=D), relu=True)
            V.memset(acc[:], 0.0).then_inc(tab_ready, 1)

            def take_slots(o):
                dve.wait_ge(slots_back, 16 * (o + 1))
                V.tensor_copy(gidx[o][:], sm3[:, :, 0])
                V.tensor_copy(local[o][:], sm3[:, :, 1]).then_inc(slots_split, 1)
                dve.wait_ge(slots_split, o + 1)

            take_slots(BY_DST)

            def build_onehot(p, t, half):
                dve.wait_ge(tile_summed, t + (p * T + SPAN - CH))
                V.tensor_tensor(onehot[:, half * CH:(half + 1) * CH, :], rowcast(iota[:], CH),
                                bcast(local[PASSES[p][0]][:, bass.ds(t, CH)], P), ALU.is_equal).then_inc(onehot_ready, CH)

            def add_tiles(p, t):
                order, w = PASSES[p][0], PASSES[p][3]
                _, at = nc.values_load_multi_w_load_instructions(
                    acc_at[order][0:1, bass.ds(t, CH)], engines=[nc.vector.engine], min_val=0, max_val=(NT - 1) * AW)
                for k in range(CH):
                    if k % 2 == 0:
                        dve.wait_ge(tile_summed, t + (p * T + SPAN + k + 2))
                    dve.wait_ge(tile_added, t + (p * T + CH + k))
                    a = accflat[:, bass.ds(at[k], w)]
                    V.tensor_tensor(a, sums[:, k, 0:w], a, ALU.add).then_inc(tile_added, 1)

            def simple_pass(p):
                with dve.Fori(0, T // SPAN) as turn:
                    t = turn * SPAN
                    for c in range(0, RING, 2):
                        build_onehot(p, t + c * CH, 0)
                        build_onehot(p, t + (c + 1) * CH, 1)
                        add_tiles(p, t + c * CH)
                        add_tiles(p, t + (c + 1) * CH)
                dve.wait_ge(tile_added, (p + 1) * T + CH)

            def inverse_counts(o):
                link(V.tensor_scalar(small[:, 0, 0:NT], acc[:, :, D], 1.0, None, ALU.max))
                link(V.reciprocal(small[:, 1, 0:NT], small[:, 0, 0:NT]))
                link(V.tensor_scalar(small[:, 0, 0:NT], acc[:, :, D], 1.0, None, ALU.min))
                link(V.tensor_tensor(inv[o][:], small[:, 1, 0:NT], small[:, 0, 0:NT], ALU.mult))

            def edge_means(p, w):
                link(V.tensor_tensor(tab[:, :, 0:w], acc[:, :, 0:w], bcast(inv[BY_DST][:], w), ALU.mult))
                V.memset(acc[:], 0.0).then_inc(tab_ready, 1)

            def batch_norm(gcol, name, count):
                wait_phase(dve, name, count)
                for o in range(2):
                    for i, (a, m) in enumerate(SPANS):
                        m = min(m, N - a)
                        ins = V.bn_stats(stats[:, o, i, :], hT[:, o, a:a + m])
                link(ins)
                for o in range(2):
                    ins = V.bn_aggr(mv[:, o, :], stats[:, o, :, :].rearrange("p a b -> p (a b)"))
                link(ins)
                V.tensor_scalar(bn[:, 0, :], mv[:, :, 1], 1.0, LN_EPS, ALU.mult, ALU.add).then_inc(act_needs, 1)
                wait_act()
                link(V.reciprocal(bn[:, 2, :], bn[:, 1, :]))
                link(V.tensor_tensor(bn[:, 2, :], bn[:, 2, :], cols[:, gcol, :], ALU.mult))
                for o in range(2):
                    ins = V.tensor_scalar(hT[:, o, :], hT[:, o, :], mv[:, o, 0:1], bn[:, 2, o:o + 1], ALU.subtract, ALU.mult)
                link(ins)
                for o in range(2):
                    ins = V.tensor_scalar(hT[:, o, :], hT[:, o, :], cols[:, gcol + 1, o:o + 1], None, ALU.add)
                ins.then_inc(mm_input, 1)

            dve.wait_ge(ones_col, 1)
            simple_pass(0)
            inverse_counts(BY_DST)
            edge_means(1, D)
            take_slots(BY_SRC)
            simple_pass(1)
            inverse_counts(BY_SRC)
            V.tensor_tensor(h[:], acc[:, :, 0:D], bcast(inv[BY_SRC][:], D), ALU.mult).then_inc(mm_input, 1)
            dve.wait_ge(loaded_w, 16 * WEIGHT_LOADS)
            batch_norm(1, "w1", 14)
            V.memset(acc[:], 0.0)
            wait_phase(dve, "t2", 13)
            link(V.memset(small[:, 7, 0:1], 0.0))
            V.memset(small[:, 7, 0:1], 0.0).then_inc(tab_ready, 1)
            simple_pass(2)
            edge_means(3, HID)
            simple_pass(3)
            link(V.tensor_tensor(tab[:], acc[:], bcast(inv[BY_SRC][:], HID), ALU.mult))
            link(V.tensor_tensor(tab[:], tab[:], rowcast(rows[:, 0:HID], NT), ALU.add))
            V.tensor_scalar(tab[:], tab[:], 0.0, None, ALU.max).then_inc(mm_input, 1)
            batch_norm(3, "r2", 13)
            V.memset(acc[:], 0.0)
            wait_phase(dve, "x3", 7)
            V.memset(small[:, 7, 0:1], 0.0).then_inc(tab_ready, 1)
            simple_pass(4)
            edge_means(5, D)
            simple_pass(5)
            link(V.tensor_tensor(h[:], acc[:, :, 0:D], bcast(inv[BY_SRC][:], D), ALU.mult))
            link(V.tensor_tensor(h[:], h[:], rowcast(rows[:, HID:HID + D], NT), ALU.add))
            link(V.tensor_scalar(h[:], h[:], 0.0, None, ALU.max))
            link(V.tensor_tensor(xres[:], xres[:], h[:], ALU.add))
            link(V.tensor_copy(h[:], xres[:]))
            layer_norm(h[:], tab[:, :, 0:D], relu=True)
            V.memset(acc[:], 0.0).then_inc(mm_input, 1)
            for l in range(LAYERS):
                p, base = 6 + l, l * T
                for j in range(NT):
                    n = FIRST[f"qkv{l}"] + j
                    wait_filled(dve, n)
                    V.tensor_tensor(q[:, j * D:(j + 1) * D], bank(n)[:, 0:D], lrow[l][:, 0, :], ALU.add)
                    V.tensor_tensor(tab[:, j, :], bank(n)[:, D:3 * D],
                                    lrow[l][:, 1:3, :].rearrange("p a b -> p (a b)"), ALU.add).then_inc(bank_free[n % 4], 1)
                wait_phase(dve, f"qkv{l}", NT)
                V.memset(small[:, 7, 0:1], 0.0).then_inc(tab_ready, 1)

                def score(t, c):
                    dve.wait_ge(q_rows, t + (base + CH))
                    first = t - c * CH
                    dve.wait_ge(gathered[c], first * 4 + (p * T * 4 + CH * 16))
                    g = G[:, c * CH:(c + 1) * CH, :]
                    s = g[:, :, 2 * D:2 * D + H]
                    V.tensor_tensor(g[:, :, 0:D], q_edge, g[:, :, 0:D], ALU.mult).then_inc(scored, CH)
                    dve.wait_ge(scored, t + (base + CH))
                    V.tensor_reduce(s, g[:, :, 0:D].rearrange("p k (h d) -> p k h d", h=H), AX.X, ALU.add).then_inc(s_chain, CH)
                    dve.wait_ge(s_chain, t + (base + CH))
                    V.tensor_scalar(s, s, CLIP, -CLIP, ALU.min, ALU.max).then_inc(clipped, CH)

                def weigh_values(t, c):
                    dve.wait_ge(weighted, t + (base + CH))
                    g = G[:, c * CH:(c + 1) * CH, :]
                    for k in range(CH):
                        v = g[:, k, D:2 * D].rearrange("p (h d) -> p h d", h=H)
                        ins = V.tensor_tensor(v, v, bcast(g[:, k, 2 * D:2 * D + H], D // H), ALU.mult)
                    ins.then_inc(messages, CH)

                build_onehot(p, 0, 0)

                def step(t, c, before=True, more=True):
                    if more:
                        build_onehot(p, t + CH, (c + 1) % 2)
                    score(t, c)
                    if before:
                        add_tiles(p, t - CH)
                    weigh_values(t, c)

                step(0, 0, before=False)
                with dve.Fori(0, (T - SPAN) // SPAN) as turn:
                    t = turn * SPAN
                    for k in range(1, RING + 1):
                        step(t + k * CH, k % RING)
                step(T - 3 * CH, 1)
                step(T - 2 * CH, 2)
                step(T - CH, 3, more=False)
                add_tiles(p, T - CH)
                dve.wait_ge(tile_added, (p + 1) * T + CH)
                link(V.tensor_scalar(z_inv[:], acc[:, :, D:D + H], 1e-6, None, ALU.add))
                link(V.reciprocal(z_inv[:], z_inv[:]))
                dve.wait_ge(tab_written[p], 16)
                for j in range(NT):
                    ins = V.tensor_tensor(tab[:, j, 0:D].rearrange("p (h d) -> p h d", h=H),
                                          acc[:, j, 0:D].rearrange("p (h d) -> p h d", h=H),
                                          bcast(z_inv[:, j, :], D // H), ALU.mult)
                ins.then_inc(mm_input, 1)
                for g, tiles in enumerate(QUADS):
                    n = FIRST[f"wo{l}"] + g
                    wait_filled(dve, n)
                    hh = h[:, tiles[0]:tiles[-1] + 1, :]
                    V.tensor_tensor(hh, bank(n)[:, 0:len(tiles) * P].rearrange("p (j c) -> p j c", c=P), hh,
                                    ALU.add).then_inc(bank_free[n % 4], 1)
                wait_phase(dve, f"wo{l}", 7)
                link(V.tensor_tensor(h[:], h[:], rowcast(lrow[l][:, 3, :], NT), ALU.add))
                layer_norm(h[:], tab[:, :, 0:D], lrow[l][:, 4, :], lrow[l][:, 5, :])
                V.memset(acc[:], 0.0).then_inc(mm_input, 1)
                for g, tiles in enumerate(QUADS):
                    n = FIRST[f"f2{l}"] + g
                    wait_filled(dve, n)
                    hh = h[:, tiles[0]:tiles[-1] + 1, :]
                    V.tensor_tensor(hh, bank(n)[:, 0:len(tiles) * P].rearrange("p (j c) -> p j c", c=P), hh,
                                    ALU.add).then_inc(bank_free[n % 4], 1)
                wait_phase(dve, f"f2{l}", 7)
                link(V.tensor_tensor(h[:], h[:], rowcast(lrow[l][:, 6, :], NT), ALU.add))
                layer_norm(h[:], tab[:, :, 0:D], lrow[l][:, 7, :], lrow[l][:, 8, :])
                if l + 1 < LAYERS:
                    V.memset(small[:, 7, 0:1], 0.0).then_inc(mm_input, 1)
            V.tensor_tensor(h[:], h[:], xres[:], ALU.add).then_inc(final_ready, 1)

        @block.tensor
        def _(pe):
            inputs = [0]

            def wait_input():
                inputs[0] += 1
                pe.wait_ge(mm_input, inputs[0])

            MM = nc.tensor.matmul
            pe.sem_inc(tile_summed, SPAN)
            pe.sem_inc(tile_added, CH)
            pe.wait_ge(consts_ready, 1)
            for o in range(2):
                pe.wait_ge(counted, o + 1)
                MM(PB[:, 7, 0:NT], below[:], small[:, 0, 0:NT], start=True, stop=True)
                MM(PB[:, 7, 64:64 + NT], ones[:], small[:, 0, 0:NT], start=True, stop=True).then_inc(counts_summed, 1)

            def sum_tiles(p, t, c):
                w = PASSES[p][3]
                for k in range(CH):
                    if k % 2 == 0:
                        pe.wait_ge(tile_added, t + (p * T + k + 2))
                    a = G[:, c * CH + k, 0:w] if p < 6 else G[:, c * CH + k, D:D + w]
                    MM(sums[:, k, 0:w], onehot[:, (c % 2) * CH + k, :], a, start=True, stop=True).then_inc(tile_summed, 1)

            def simple_pass(p):
                with pe.Fori(0, T // SPAN) as turn:
                    t = turn * SPAN
                    for c in range(RING):
                        pe.wait_ge(onehot_ready, t + (p * T + (c + 1) * CH))
                        pe.wait_ge(gathered[c], t * 4 + (p * T * 4 + CH * 16))
                        sum_tiles(p, t + c * CH, c)

            def group(n, products):
                if n >= 4:
                    wait_evacuated(pe, n - 4)
                for a, b, lhsT, rhs, start, stop in products:
                    last = MM(bank(n)[:, a:b], lhsT, rhs, start=start, stop=stop)
                last.then_inc(group_ready, 1)

            def transposes(n, tiles):
                if n >= 4:
                    wait_evacuated(pe, n - 4)
                for i, ap in enumerate(tiles):
                    last = nc.tensor.transpose(bank(n)[:, i * P:(i + 1) * P], ap, ident[:])
                last.then_inc(group_ready, 1)

            def transpose_nodes(name, source):
                for g, tiles in enumerate(QUADS):
                    transposes(FIRST[name] + g, [source[:, j, 0:D] for j in tiles])

            def cols_of(j):
                return slice(j * P, (j + 1) * P)

            pe.wait_ge(ones_col, 1)
            simple_pass(0)
            simple_pass(1)
            pe.wait_ge(loaded_w, 16 * WEIGHT_LOADS)
            wait_input()
            transpose_nodes("z1", h)
            wait_phase(pe, "z1", 7)
            for i, (o, (a, m)) in enumerate((o, s) for o in range(2) for s in SPANS):
                group(FIRST["w1"] + i, [(0, m, W1_s[:, o * P:(o + 1) * P], zT[:, a:a + m], True, True)])
            wait_input()
            for g, tiles in enumerate(PAIRS):
                group(FIRST["t2"] + g, [(i * 256, i * 256 + 256, hT[:, k, cols_of(j)], W2_s[:, k, :], k == 0, k == 1)
                                        for i, j in enumerate(tiles) for k in range(2)])
            simple_pass(2)
            simple_pass(3)
            wait_input()
            for g, tiles in enumerate(PAIRS):
                transposes(FIRST["r2"] + g, [tab[:, j, o * P:(o + 1) * P] for o in range(2) for j in tiles])
            wait_input()
            for g, tiles in enumerate(QUADS):
                group(FIRST["x3"] + g, [(i * P, i * P + P, hT[:, k, cols_of(j)], W3_s[:, k, :], k == 0, k == 1)
                                        for i, j in enumerate(tiles) for k in range(2)])
            simple_pass(4)
            simple_pass(5)
            wait_input()
            transpose_nodes("h", h)
            wait_phase(pe, "h", 7)
            for g, tiles in enumerate(QUADS):
                group(FIRST["emb"] + g, [(i * P, i * P + P, zT[:, cols_of(j)], Wemb_s[:], True, True)
                                         for i, j in enumerate(tiles)])
            for g, (a, m) in enumerate(SPANS):
                group(FIRST["embT"] + g, [(0, m, Wemb_s[:], zT[:, a:a + m], True, True)])
            for l in range(LAYERS):
                p, base = 6 + l, l * T
                wait_phase(pe, "embT" if l == 0 else f"nx{l - 1}", 7)
                for j in range(NT):
                    group(FIRST[f"qkv{l}"] + j,
                          [(0, 3 * D, sT[:, cols_of(j)], Wqkv_s[l][:].rearrange("p a b -> p (a b)"), True, True)])
                wait_phase(pe, f"qkv{l}", NT)

                def expand(t, c):
                    pe.wait_ge(onehot_ready, t + (p * T + CH))
                    if not (l == 0 and isinstance(t, int) and t == 0):
                        pe.wait_ge(ohT_ready, t + base)
                    for k in range(CH):
                        last = nc.tensor.transpose(ohT_ps[:, k, :], onehot[:, (c % 2) * CH + k, :], ident[:])
                    last.then_inc(ohT_in_psum, CH)
                    _, at = nc.values_load_multi_w_load_instructions(
                        q_at[0:1, bass.ds(t, CH)], engines=[nc.tensor.engine], min_val=0, max_val=(NT - 1) * D)
                    pe.wait_ge(ohT_ready, t + (base + CH))
                    if not (l == 0 and isinstance(t, int) and t == 0):
                        pe.wait_ge(scored, t + base)
                    for k in range(CH):
                        last = MM(q_edge[:, k, :], onehotT[:, k, :], q[:, bass.ds(at[k], D)], start=True, stop=True)
                    last.then_inc(q_rows, CH)

                expand(0, 0)

                def step(t, c, more=True):
                    if more:
                        expand(t + CH, (c + 1) % 2)
                    pe.wait_ge(messages, t + (base + CH))
                    sum_tiles(p, t, c)

                step(0, 0)
                with pe.Fori(0, (T - SPAN) // SPAN) as turn:
                    t = turn * SPAN
                    for k in range(1, RING + 1):
                        step(t + k * CH, k % RING)
                step(T - 3 * CH, 1)
                step(T - 2 * CH, 2)
                step(T - CH, 3, more=False)
                wait_input()
                transpose_nodes(f"at{l}", tab)
                wait_phase(pe, f"at{l}", 7)
                for g, tiles in enumerate(QUADS):
                    group(FIRST[f"wo{l}"] + g, [(i * P, i * P + P, zT[:, cols_of(j)], Wo_s[l][:], True, True)
                                                for i, j in enumerate(tiles)])
                wait_input()
                transpose_nodes(f"hx{l}", h)
                wait_phase(pe, f"hx{l}", 7)
                for i, (o, (a, m)) in enumerate((o, s) for o in range(2) for s in SPANS):
                    group(FIRST[f"f1{l}"] + i, [(0, m, Wf1_s[l][:, o * P:(o + 1) * P], zT[:, a:a + m], True, True)])
                wait_phase(pe, f"f1{l}", 14)
                for g, tiles in enumerate(QUADS):
                    group(FIRST[f"f2{l}"] + g, [(i * P, i * P + P, hT[:, k, cols_of(j)], Wf2_s[l][:, k, :], k == 0, k == 1)
                                                for i, j in enumerate(tiles) for k in range(2)])
                if l + 1 < LAYERS:
                    wait_input()
                    transpose_nodes(f"nx{l}", h)


WEIGHT_LOADS = 4 + 5 + 2 + LAYERS * (3 + 4 + 9)

_INS = ['x', 'src', 'dst', 'L0_gnn_W1', 'L0_gnn_b1', 'L0_gnn_g1', 'L0_gnn_be1', 'L0_gnn_W2', 'L0_gnn_b2', 'L0_gnn_g2',
        'L0_gnn_be2', 'L0_gnn_W3', 'L0_gnn_b3', 'L1_gnn_W_emb', 'L1_gnn_Wq', 'L1_gnn_bq', 'L1_gnn_Wk', 'L1_gnn_bk',
        'L1_gnn_Wv', 'L1_gnn_bv', 'L1_gnn_Wo', 'L1_gnn_bo', 'L1_gnn_ln1_w', 'L1_gnn_ln1_b', 'L1_gnn_Wf1', 'L1_gnn_bf1',
        'L1_gnn_Wf2', 'L1_gnn_bf2', 'L1_gnn_ln2_w', 'L1_gnn_ln2_b']


def kernel(**inputs):
    import numpy as _np
    import concourse.bacc as _bacc
    from concourse import mybir as _mybir
    from concourse.bass_utils import run_bass_kernel_spmd as _run

    nc = _bacc.Bacc("TRN2", target_bir_lowering=False, num_devices=1)
    arrays, args = {}, []
    for name in _INS:
        a = _np.ascontiguousarray(inputs[name])
        arrays[f"in_{name}_dram"] = a
        args.append(nc.dram_tensor(f"in_{name}_dram", a.shape, _mybir.dt.from_np(a.dtype), kind="ExternalInput").ap())
    args.append(nc.dram_tensor("out_0_dram", (N, D), f32, kind="ExternalOutput").ap())
    build(nc, *args)
    r = _run(nc, [arrays], core_ids=[0])
    return r.results[0]["out_0_dram"]
```
